# Optimizing a Trainium2 kernel written in Bass

```python
import numpy as np
import jax
import jax.numpy as jnp

def _softmax(x, axis=-1):
    return jax.nn.softmax(x, axis=axis)

def _gelu(x):
    return jax.nn.gelu(x, approximate=True)

def _silu(x):
    return jax.nn.silu(x)

def _sigmoid(x):
    return jax.nn.sigmoid(x)

def _layernorm(x, axis=-1, eps=1e-05):
    m = jnp.mean(x, axis=axis, keepdims=True)
    v = jnp.var(x, axis=axis, keepdims=True)
    return (x - m) / jnp.sqrt(v + eps)

def _scatter_add(tgt, idx, src, axis=0):
    return tgt.at[idx].add(src)

def _segment_sum(src, seg, n):
    return jax.ops.segment_sum(src, seg, n)
kernel_name = 'mk_adaln_ffn_d1_seqx_r8_664633'

def setup_inputs(seed: int=0):
    np.random.seed(seed)
    _w = jnp.asarray

    def _rec_inputs():
        import jax
        import jax.numpy as jnp
        _rk = jax.random.key(seed)
        x = -7.109e-05 + 0.9999 * jax.random.normal(jax.random.fold_in(_rk, 1), (64, 32, 512), jnp.float32)
        _lenS = 32 - jax.random.randint(jax.random.fold_in(_rk, 7), (64,), 0, max(1, 32 // 4) + 1, jnp.int32)
        _lenS2 = 32 - jax.random.randint(jax.random.fold_in(_rk, 8), (64,), 0, max(1, 32 // 4) + 1, jnp.int32)
        itok_B_0_30 = jax.random.randint(jax.random.fold_in(_rk, 11), (64,), 0, 31, jnp.int32)
        return (x, itok_B_0_30)
    x, itok_B_0_30 = _rec_inputs()

    def _L0_cond_setup():
        import jax, jax.numpy as jnp
        import numpy as np
        B, C, D, T, S = (64, 32, 32, 512, 32)
        key = jax.random.key(seed)
        k1, k2, k3 = jax.random.split(key, 3)
        x = jax.random.normal(k1, (B, C, T), dtype=jnp.float32)
        subjects = jax.random.randint(k2, (B,), 0, S, dtype=jnp.int64)
        weights = jax.random.normal(k3, (S, C, D), dtype=jnp.float32) * (1.0 / np.sqrt(C))
        return {'x': x, 'subjects': subjects, 'weights': weights}
    _L0_cond_all = _L0_cond_setup()
    _L0_cond_in = {k: v for k, v in _L0_cond_all.items() if k in ('weights',)}
    del _L0_cond_all

    def _L0_ffn_setup():
        import jax, jax.numpy as jnp
        import numpy as np
        RANKS = (8, 16, 32, 64)
        TOPK = 1
        SCALING = 1.0 / 4
        key = jax.random.key(seed)
        ks = jax.random.split(key, 7)
        D_IN, D_OUT, MAX_R, N_RANKS = (512, 512, 64, len(RANKS))
        B_, S_ = (4, 256)
        return {'hidden_states': jax.random.normal(ks[0], (B_, S_, D_IN), jnp.float32), 'W': jax.random.normal(ks[1], (D_OUT, D_IN), jnp.float32) * 0.02, 'b': jax.random.normal(ks[2], (D_OUT,), jnp.float32) * 0.02, 'A': jax.random.normal(ks[3], (MAX_R, D_IN), jnp.float32) * 0.02, 'B': jnp.zeros((D_OUT, MAX_R), jnp.float32) + jax.random.normal(ks[4], (D_OUT, MAX_R), jnp.float32) * 0.02, 'gate_w': jax.random.normal(ks[5], (N_RANKS, D_IN), jnp.float32) * 0.02, 'gate_b': jax.random.normal(ks[6], (N_RANKS,), jnp.float32) * 0.02}
    _L0_ffn_all = _L0_ffn_setup()
    _L0_ffn_in = {k: v for k, v in _L0_ffn_all.items() if k in ('W', 'b', 'A', 'B', 'gate_w', 'gate_b')}
    del _L0_ffn_all
    return {'x': x, 'itok_B_0_30': itok_B_0_30, 'L0_cond_weights': _L0_cond_in['weights'], 'L0_ffn_W': _L0_ffn_in['W'], 'L0_ffn_b': _L0_ffn_in['b'], 'L0_ffn_A': _L0_ffn_in['A'], 'L0_ffn_B': _L0_ffn_in['B'], 'L0_ffn_gate_w': _L0_ffn_in['gate_w'], 'L0_ffn_gate_b': _L0_ffn_in['gate_b']}

def reference(x, itok_B_0_30, L0_cond_weights, L0_ffn_W, L0_ffn_b, L0_ffn_A, L0_ffn_B, L0_ffn_gate_w, L0_ffn_gate_b):
    import jax
    import jax.numpy as jnp

    def _L0_cond_ref(x, subjects, weights):
        import jax, jax.numpy as jnp
        import numpy as np
        B, C, D, T, S = (64, 32, 32, 512, 32)
        w = weights[subjects]
        return jnp.einsum('bct,bcd->bdt', x, w)

    def _L0_ffn_ref(hidden_states, W, b, A, B, gate_w, gate_b):
        import jax, jax.numpy as jnp
        import numpy as np
        RANKS = (8, 16, 32, 64)
        TOPK = 1
        SCALING = 1.0 / 4
        bsz, seq, d_in = hidden_states.shape
        out = jnp.einsum('bsd,od->bso', hidden_states, W) + b
        x = hidden_states.reshape(-1, d_in)
        scores = x @ gate_w.T + gate_b
        probs = jax.nn.softmax(scores, axis=-1)
        routing_weights, selected = jax.lax.top_k(probs, TOPK)
        routing_weights = routing_weights / jnp.sum(routing_weights, axis=-1, keepdims=True)
        lora_outputs = jnp.stack([x @ A[:r, :].T @ B[:, :r].T for r in RANKS], axis=1)
        sel = jnp.take_along_axis(lora_outputs, selected[:, :, None], axis=1)
        final = jnp.sum(sel * routing_weights[:, :, None], axis=1)
        return out + final.reshape(bsz, seq, -1)
    x = x + _L0_ffn_ref(_L0_cond_ref(x, itok_B_0_30, L0_cond_weights), L0_ffn_W, L0_ffn_b, L0_ffn_A, L0_ffn_B, L0_ffn_gate_w, L0_ffn_gate_b)
    return x

_drawn_inputs = setup_inputs


def setup_inputs(seed=0):
    import zlib

    import numpy as np

    out = dict(_drawn_inputs(seed))
    spreads = {}
    factors = {'L0_ffn_b': 3.188, 'L0_ffn_gate_b': 27.801}
    for name, (base, spread) in spreads.items():
        noise = np.random.default_rng([zlib.crc32(name.encode()), seed]).standard_normal(out[name].shape)
        drawn = base * np.exp(spread * noise) if base else spread * noise
        out[name] = jnp.asarray(drawn.astype(out[name].dtype))
    for name, factor in factors.items():
        out[name] = (out[name] * factor).astype(out[name].dtype)
    return out
```

```python
import concourse.bass as bass
from concourse import mybir
from contextlib import ExitStack


def bass_adaln_ffn_kernel(
    nc: bass.Bass,
    x: bass.AP,
    subject: bass.AP,
    cond_w: bass.AP,
    wag: bass.AP,
    lora_bt: bass.AP,
    lin_b: bass.AP,
    gate_b: bass.AP,
    out: bass.AP,
):
    f32 = mybir.dt.float32
    f32r = mybir.dt.float32r
    i32 = mybir.dt.int32
    ALU = mybir.AluOpType
    ACT = mybir.ActivationFunctionType
    AX = mybir.AxisListType

    P = 128
    NB, C, T = x.shape
    QB = P // C
    NG = NB // QB
    KT = T // P
    R = lora_bt.shape[0]
    NR = gate_b.shape[1]
    RANKS = (8, 16, 32, 64)
    COLS = T + R + NR
    HALF = T // 2
    BANK = 512
    TAIL = COLS - HALF
    UN = 4
    LAST = NG // UN - 1

    x_rows = x.rearrange("b c t -> (b c) t")
    out_rows = out.rearrange("b c t -> (b c) t")
    w_rows = cond_w.rearrange("s c d -> (s c) d")

    ctx = ExitStack()
    with ctx:
        def sb(name, shape, dt=f32):
            return ctx.enter_context(nc.sbuf_tensor(name, shape, dt))

        def pb(name, shape):
            return ctx.enter_context(nc.psum_tensor(name, shape, f32))

        def sem(name):
            return ctx.enter_context(nc.semaphore(name))

        x_sb = [sb(f"x_sb{i}", [P, T]) for i in range(UN)]
        out_sb = [sb(f"out_sb{i}", [P, T]) for i in range(2)]
        ids = sb("ids", [P, NG], i32)
        chan = sb("chan", [P, 1], i32)
        chan_f = sb("chan_f", [P, 1])
        rows = sb("rows", [P, NG], i32)
        w_gat = [sb(f"w_gat{i}", [P, C]) for i in range(UN)]
        w_bd = [sb(f"w_bd{i}", [P, P]) for i in range(UN)]
        wag_raw = sb("wag_raw", [P, KT, COLS])
        wag_hi = sb("wag_hi", [P, KT, COLS], f32r)
        wag_lo = sb("wag_lo", [P, KT, COLS], f32r)
        bt_raw = sb("bt_raw", [P, T])
        bt_hi = sb("bt_hi", [P, T], f32r)
        bt_lo = sb("bt_lo", [P, T], f32r)
        bias_raw = sb("bias_raw", [P, T])
        bias_hi = sb("bias_hi", [P, T])
        gate_bias = sb("gate_bias", [P, NR])
        ident = sb("ident", [P, P])
        block_no = sb("block_no", [P, R])
        order = sb("order", [P, NR])
        h_hi = [sb(f"h_hi{i}", [P, T], f32r) for i in range(2)]
        h_lo = [sb(f"h_lo{i}", [P, T], f32r) for i in range(2)]
        score = sb("score", [P, NR])
        top = sb("top", [P, 1])
        shifted = [sb(f"shifted{i}", [P, NR]) for i in range(2)]
        picked = sb("picked", [P, NR])
        first = sb("first", [P, 1])
        expd = [sb(f"expd{i}", [P, NR]) for i in range(2)]
        expsum = [sb(f"expsum{i}", [P, 1]) for i in range(2)]
        inv_sum = sb("inv_sum", [P, 1])
        prob = sb("prob", [P, NR])
        prob_top = sb("prob_top", [P, 1])
        inv_top = sb("inv_top", [P, 1])
        mask = sb("mask", [P, R])
        u_raw = sb("u_raw", [P, R])
        u_sel = [sb(f"u_sel{i}", [P, 2 * R]) for i in range(2)]
        u_hilo = sb("u_hilo", [P, P], f32r)
        u_one = sb("u_one", [P, P], f32r)

        h_ps = [pb(f"h_ps{i}", [P, T]) for i in range(2)]
        acc = [pb(f"acc{i}", [P, 2 * BANK]) for i in range(2)]
        u_ps = pb("u_ps", [P, BANK])
        Y0 = BANK - HALF
        U0 = Y0 + T
        S0 = U0 + R

        ids_in = sem("ids_in")
        wag_in = [sem(f"wag_in{k}") for k in range(KT)]
        bt_in = sem("bt_in")
        bias_in = sem("bias_in")
        gate_in = sem("gate_in")
        x_in = [sem(f"x_in{i}") for i in range(UN)]
        stored = [sem(f"stored{i}") for i in range(2)]
        gathered = [sem(f"gathered{i}") for i in range(UN)]
        chan_made = sem("chan_made")
        rows_made = sem("rows_made")
        zeroed = sem("zeroed")
        w_ready = sem("w_ready")
        const_made = sem("const_made")
        u_one_made = sem("u_one_made")
        bt_zeroed = sem("bt_zeroed")
        wag_hi_made = sem("wag_hi_made")
        wag_lo_made = sem("wag_lo_made")
        bt_hi_made = sem("bt_hi_made")
        bt_lo_made = sem("bt_lo_made")
        mixed = sem("mixed")
        h_hi_made = sem("h_hi_made")
        h_lo_made = sem("h_lo_made")
        main_done = sem("main_done")
        shift_made = sem("shift_made")
        exp_done = sem("exp_done")
        route_step = sem("route_step")
        u_sel_made = sem("u_sel_made")
        u_turned = sem("u_turned")
        u_copied = sem("u_copied")
        y_ready = sem("y_ready")
        added = sem("added")

        def at(n, r):
            return n + r // UN, r % UN

        def count(n, r):
            return n * UN + r

        block = ctx.enter_context(nc.Block())

        @block.sync
        def _(sp):
            def load_x(n, r):
                sp.dma_start(x_sb[r][:, :], x_rows[bass.ds(count(n, r) * P, P), :]).then_inc(x_in[r], 16)

            for q in range(QB):
                sp.dma_start(ids[q * C:(q + 1) * C, :], subject[q:q + 1, :].to_broadcast([C, NG])).then_inc(ids_in, 16)
            load_x(0, 0)
            for k in range(KT):
                sp.dma_start(wag_raw[:, k, :], wag[k * P:(k + 1) * P, :]).then_inc(wag_in[k], 16)
            load_x(0, 1)
            sp.dma_start(gate_bias[:, :], gate_b.to_broadcast([P, NR])).then_inc(gate_in, 16)
            sp.dma_start(bt_raw[0:R, :], lora_bt[:, :]).then_inc(bt_in, 16)
            sp.dma_start(bt_raw[R:2 * R, :], lora_bt[:, :]).then_inc(bt_in, 16)
            sp.dma_start(bias_raw[64:65, :], lin_b[:, :]).then_inc(bias_in, 16)
            sp.dma_start(bias_raw[96:97, :], lin_b[:, :]).then_inc(bias_in, 16)
            load_x(0, 2)
            load_x(0, 3)

            def store(n, r):
                sp.wait_ge(added, count(n, r) + 1)
                sp.dma_start(out_rows[bass.ds(count(n, r) * P, P), :], out_sb[r % 2][:, :]).then_inc(stored[r % 2], 16)

            with sp.Fori(0, LAST) as n:
                for r in range(UN):
                    store(n, r)
                    load_x(n + 1, r)
            for r in range(UN):
                store(NG // UN - 1, r)
            for i in range(2):
                sp.wait_ge(stored[i], 16 * NG // 2)

        @block.gpsimd
        def _(pool):
            for q in range(QB):
                pool.iota(chan[q * C:(q + 1) * C, :], pattern=[[0, 1]], base=0, channel_multiplier=1).then_inc(chan_made, 1)
            pool.wait_ge(chan_made, QB)
            pool.memset(ident[:, :], 0.0).then_inc(const_made, 1)
            pool.wait_ge(const_made, 1)
            pool.affine_select(out=ident[:, :], in_=ident[:, :], compare_op=ALU.not_equal, fill=1.0,
                               base=0, pattern=[[-1, P]], channel_multiplier=1).then_inc(const_made, 1)
            pool.wait_ge(const_made, 2)

            def gather(g):
                pool.indirect_dma_start(w_gat[g % UN][:, :], None, w_rows,
                                        bass.IndirectOffsetOnAxis(ap=rows[:, g:g + 1], axis=0)).then_inc(gathered[g % UN], 16)

            pool.wait_ge(rows_made, 1)
            for g in range(NG):
                if g >= UN:
                    pool.wait_ge(w_ready, QB * (g - UN + 1))
                gather(g)

        @block.scalar
        def _(act):
            def spread(n, r, reused):
                act.wait_ge(gathered[r], 16 * (n + 1))
                if reused:
                    act.wait_ge(mixed, count(n, r) - UN + 1)
                for q in range(QB):
                    s = slice(q * C, (q + 1) * C)
                    act.activation(w_bd[r][s, s], w_gat[r][s, :], ACT.Copy).then_inc(w_ready, 1)

            for k in range(KT):
                act.wait_ge(wag_in[k], 16)
                act.activation(wag_hi[:, k, :], wag_raw[:, k, :], ACT.Copy).then_inc(wag_hi_made, 1)

            def h_high(n, r, reused):
                act.wait_ge(mixed, count(n, r) + 1)
                if reused:
                    act.wait_ge(main_done, count(n, r) - 1)
                act.activation(h_hi[r % 2][:, :], h_ps[r % 2][:, :], ACT.Copy).then_inc(h_hi_made, 1)

            def exps(n, r):
                act.wait_ge(shift_made, count(n, r) + 1)
                act.activation(expd[r % 2][:, :], shifted[r % 2][:, :], ACT.Exp,
                               accum_out=expsum[r % 2][:, :]).then_inc(exp_done, 1)

            def u_out(n, r, reused):
                act.wait_ge(u_turned, count(n, r) + 1)
                if reused:
                    act.wait_ge(y_ready, count(n, r))
                act.activation(u_hilo[:, :], u_ps[:, 0:P], ACT.Copy).then_inc(u_copied, 1)
                act.activation(u_one[0:R, :], u_ps[0:R, 0:P], ACT.Copy).then_inc(u_copied, 1)

            act.wait_ge(zeroed, UN)
            spread(0, 0, False)
            spread(0, 1, False)
            h_high(0, 0, False)
            h_high(0, 1, False)
            act.wait_ge(bt_in, 32)
            act.activation(bt_hi[:, :], bt_raw[:, :], ACT.Copy).then_inc(bt_hi_made, 1)
            act.wait_ge(bias_in, 32)
            act.wait_ge(bt_zeroed, 1)
            act.activation(bt_lo[64:65, :], bias_raw[64:65, :], ACT.Copy).then_inc(bt_hi_made, 1)
            act.activation(bias_hi[96:97, :].bitcast(f32r), bias_raw[96:97, :], ACT.Copy).then_inc(bt_hi_made, 1)

            def slot(n, r, wbd_reused, u_reused):
                spread(*at(n, r + 1), wbd_reused)
                exps(*at(n, r - 1))
                h_high(*at(n, r + 1), True)
                u_out(*at(n, r - 1), u_reused)

            slot(0, 1, False, False)
            slot(0, 2, False, True)
            with act.Fori(0, LAST) as n:
                for r in range(3, 3 + UN):
                    slot(n, r, True, True)
            for r in (UN - 2, UN - 1):
                exps(LAST, r)
                u_out(LAST, r, True)

        @block.tensor
        def _(pe):
            def mix(n, r, reused):
                pe.wait_ge(x_in[r], 16 * (n + 1))
                pe.wait_ge(w_ready, QB * (count(n, r) + 1))
                if reused:
                    pe.wait_ge(h_lo_made, count(n, r) - 1)
                for k in range(KT):
                    mm = pe.matmul(h_ps[r % 2][:, k * P:(k + 1) * P], x_sb[r][:, k * P:(k + 1) * P], w_bd[r][:, :],
                                   start=True, stop=True)
                mm.then_inc(mixed, 1)

            def product(r, k, h, w, first_, last_):
                y = acc[r % 2]
                hk = h[r % 2][:, k * P:(k + 1) * P]
                pe.matmul(y[:, Y0:BANK], hk, w[:, k, 0:HALF], start=first_, stop=last_)
                return pe.matmul(y[:, BANK:BANK + TAIL], hk, w[:, k, HALF:COLS], start=first_, stop=last_)

            def main_high(n, r, reused, fresh):
                pe.wait_ge(h_hi_made, count(n, r) + 1)
                if reused:
                    pe.wait_ge(added, count(n, r) - 1)
                for k in range(KT):
                    if fresh:
                        pe.wait_ge(wag_hi_made, k + 1)
                    product(r, k, h_hi, wag_hi, k == 0, False)
                for k in range(KT):
                    if fresh:
                        pe.wait_ge(wag_lo_made, k + 1)
                    product(r, k, h_hi, wag_lo, False, False)

            def main_low(n, r):
                pe.wait_ge(h_lo_made, count(n, r) + 1)
                for k in range(KT):
                    mm = product(r, k, h_lo, wag_hi, False, k == KT - 1)
                mm.then_inc(main_done, 1)

            def turn(n, r, reused):
                pe.wait_ge(u_sel_made, count(n, r) + 1)
                if reused:
                    pe.wait_ge(u_copied, 2 * count(n, r))
                pe.transpose(u_ps[:, 0:P], u_sel[r % 2][:, :], ident[:, :]).then_inc(u_turned, 1)

            def lora(n, r):
                pe.wait_ge(u_copied, 2 * count(n, r) + 2)
                y = acc[r % 2]
                for u, b in ((u_hilo, bt_hi), (u_one, bt_lo)):
                    pe.matmul(y[:, Y0:BANK], u[:, :], b[:, 0:HALF], start=False, stop=False, skip_group_check=True)
                    mm = pe.matmul(y[:, BANK:BANK + HALF], u[:, :], b[:, HALF:T], start=False, stop=False,
                                   skip_group_check=True)
                mm.then_inc(y_ready, 1)

            mix(0, 0, False)
            mix(0, 1, False)
            main_high(0, 0, False, True)
            main_low(0, 0)
            pe.wait_ge(const_made, 2)
            pe.wait_ge(bt_hi_made, 3)
            pe.wait_ge(bt_lo_made, 2)

            def slot(n, r, acc_reused, u_reused):
                mix(*at(n, r + 1), True)
                main_high(*at(n, r), acc_reused, False)
                turn(*at(n, r - 1), u_reused)
                main_low(*at(n, r))
                lora(*at(n, r - 1))

            slot(0, 1, False, False)
            slot(0, 2, True, True)
            with pe.Fori(0, LAST) as n:
                for r in range(3, 3 + UN):
                    slot(n, r, True, True)
            main_high(LAST, UN - 1, True, False)
            turn(LAST, UN - 2, True)
            main_low(LAST, UN - 1)
            lora(LAST, UN - 2)
            turn(LAST, UN - 1, True)
            lora(LAST, UN - 1)

        @block.vector
        def _(dve):
            dve.wait_ge(ids_in, 16 * QB)
            dve.wait_ge(chan_made, QB)
            dve.tensor_copy(chan_f[:, :], chan[:, :]).then_inc(chan_made, 1)
            dve.wait_ge(chan_made, QB + 1)
            dve.tensor_scalar(rows[:, :], ids[:, :], float(C), chan_f[:, 0:1], ALU.mult, ALU.add).then_inc(rows_made, 1)
            for i in range(UN):
                dve.memset(w_bd[i][:, :], 0.0).then_inc(zeroed, 1)
            start = 0
            for j, end in enumerate(RANKS):
                dve.memset(block_no[:, start:end], float(NR - j)).then_inc(u_one_made, 1)
                dve.memset(order[:, j:j + 1], float(NR - j)).then_inc(u_one_made, 1)
                start = end
            dve.memset(u_one[64:96, :].bitcast(f32), 0.0).then_inc(u_one_made, 1)
            dve.memset(u_one[96:128, :].bitcast(f32), 0.0).then_inc(u_one_made, 1)
            dve.wait_ge(u_one_made, 2 * NR + 2)
            dve.memset(u_one[64:65, :].bitcast(f32), 1.0).then_inc(u_one_made, 1)
            dve.memset(u_one[96:97, :].bitcast(f32), 1.0).then_inc(u_one_made, 1)
            dve.memset(bt_lo[64:128, :].bitcast(f32), 0.0).then_inc(bt_zeroed, 1)
            for k in range(KT):
                dve.wait_ge(wag_hi_made, k + 1)
                dve.tensor_tensor(wag_lo[:, k, :], wag_raw[:, k, :], wag_hi[:, k, :].bitcast(f32),
                                  ALU.subtract).then_inc(wag_lo_made, 1)

            def h_low(n, r, reused):
                dve.wait_ge(h_hi_made, count(n, r) + 1)
                if reused:
                    dve.wait_ge(main_done, count(n, r) - 1)
                dve.tensor_tensor(h_lo[r % 2][:, :], h_ps[r % 2][:, :], h_hi[r % 2][:, :].bitcast(f32),
                                  ALU.subtract).then_inc(h_lo_made, 1)

            ROUTE_STEPS = 11

            def route(n, r):
                done = count(n, r) * ROUTE_STEPS
                a = acc[r % 2]
                dve.wait_ge(main_done, count(n, r) + 1)
                dve.tensor_tensor(score[:, :], a[:, S0:S0 + NR], gate_bias[:, :], ALU.add).then_inc(route_step, 1)
                dve.wait_ge(route_step, done + 1)
                dve.tensor_reduce(top[:, :], score[:, :], AX.X, ALU.max).then_inc(route_step, 1)
                dve.wait_ge(route_step, done + 2)
                dve.tensor_scalar(shifted[r % 2][:, :], score[:, :], top[:, 0:1], None,
                                  ALU.subtract).then_inc(shift_made, 1)
                dve.wait_ge(shift_made, count(n, r) + 1)
                dve.scalar_tensor_tensor(out=picked[:, :], in0=shifted[r % 2][:, :], scalar=0.0, in1=order[:, :],
                                         op0=ALU.is_ge, op1=ALU.mult).then_inc(route_step, 1)
                dve.wait_ge(route_step, done + 3)
                dve.tensor_reduce(first[:, :], picked[:, :], AX.X, ALU.max).then_inc(route_step, 1)
                dve.wait_ge(exp_done, count(n, r) + 1)
                dve.reciprocal(inv_sum[:, :], expsum[r % 2][:, :]).then_inc(route_step, 1)
                dve.wait_ge(route_step, done + 5)
                dve.tensor_scalar(prob[:, :], expd[r % 2][:, :], inv_sum[:, 0:1], None, ALU.mult).then_inc(route_step, 1)
                dve.wait_ge(route_step, done + 6)
                dve.tensor_reduce(prob_top[:, :], prob[:, :], AX.X, ALU.max).then_inc(route_step, 1)
                dve.wait_ge(route_step, done + 7)
                dve.reciprocal(inv_top[:, :], prob_top[:, :]).then_inc(route_step, 1)
                dve.tensor_scalar(mask[:, :], block_no[:, :], first[:, 0:1], prob_top[:, 0:1],
                                  ALU.is_ge, ALU.mult).then_inc(route_step, 1)
                dve.wait_ge(route_step, done + 9)
                dve.scalar_tensor_tensor(out=u_raw[:, :], in0=mask[:, :], scalar=inv_top[:, 0:1],
                                         in1=a[:, U0:U0 + R], op0=ALU.mult, op1=ALU.mult).then_inc(route_step, 1)
                u = u_sel[r % 2]
                dve.wait_ge(route_step, done + 10)
                dve.tensor_copy(u[:, 0:R].bitcast(f32r), u_raw[:, :]).then_inc(route_step, 1)
                dve.wait_ge(route_step, done + 11)
                dve.tensor_tensor(u[:, R:2 * R], u_raw[:, :], u[:, 0:R], ALU.subtract).then_inc(u_sel_made, 1)

            def add(n, r, reused):
                dve.wait_ge(y_ready, count(n, r) + 1)
                if reused:
                    dve.wait_ge(stored[r % 2], (n * (UN // 2) + r // 2) * 16)
                dve.tensor_tensor(out_sb[r % 2][:, :], acc[r % 2][:, Y0:Y0 + T], x_sb[r][:, :],
                                  ALU.add).then_inc(added, 1)

            h_low(0, 0, False)
            h_low(0, 1, False)
            dve.wait_ge(bt_hi_made, 3)
            dve.wait_ge(bt_zeroed, 1)
            dve.tensor_tensor(bt_lo[0:R, :], bt_raw[0:R, :], bt_hi[0:R, :].bitcast(f32), ALU.subtract).then_inc(bt_lo_made, 1)
            dve.tensor_tensor(bt_lo[96:97, :], bias_raw[96:97, :], bias_hi[96:97, :], ALU.subtract).then_inc(bt_lo_made, 1)
            dve.wait_ge(gate_in, 16)

            def slot(n, r, out_reused):
                route(*at(n, r - 1))
                h_low(*at(n, r + 1), True)
                add(*at(n, r - 1), out_reused)

            slot(0, 1, False)
            slot(0, 2, False)
            with dve.Fori(0, LAST) as n:
                for r in range(3, 3 + UN):
                    slot(n, r, True)
            for r in (UN - 2, UN - 1):
                route(LAST, r)
                add(LAST, r, True)


def kernel(x, itok_B_0_30, L0_cond_weights, L0_ffn_W, L0_ffn_b, L0_ffn_A, L0_ffn_B, L0_ffn_gate_w, L0_ffn_gate_b):
    import numpy as _np
    import concourse.bacc as _bacc
    from concourse import mybir as _mybir
    from concourse.bass_utils import run_bass_kernel_spmd as _run

    w, a, g = (_np.asarray(t) for t in (L0_ffn_W, L0_ffn_A, L0_ffn_gate_w))
    laid = {
        "x": _np.asarray(x),
        "subject": _np.asarray(itok_B_0_30).reshape(-1, 4).T,
        "cond_w": _np.asarray(L0_cond_weights),
        "wag": _np.concatenate([w.T, a.T, g.T], axis=1),
        "lora_bt": _np.asarray(L0_ffn_B).T,
        "lin_b": _np.asarray(L0_ffn_b).reshape(1, -1),
        "gate_b": _np.asarray(L0_ffn_gate_b).reshape(1, -1),
    }
    nc = _bacc.Bacc("TRN2", target_bir_lowering=False, num_devices=1)
    arrays, args = {}, []
    for name, t in laid.items():
        t = _np.ascontiguousarray(t)
        arrays[f"in_{name}_dram"] = t
        args.append(nc.dram_tensor(f"in_{name}_dram", t.shape, _mybir.dt.from_np(t.dtype), kind="ExternalInput").ap())
    args.append(nc.dram_tensor("out_0_dram", laid["x"].shape, _mybir.dt.from_np(laid["x"].dtype), kind="ExternalOutput").ap())
    bass_adaln_ffn_kernel(nc, *args)
    r = _run(nc, [arrays], core_ids=[0])
    return r.results[0]["out_0_dram"]
```

```python
import concourse.bass as bass
from concourse import mybir
from contextlib import ExitStack


def bass_adaln_ffn_kernel(
    nc: bass.Bass,
    x: bass.AP,
    subject: bass.AP,
    cond_w: bass.AP,
    wag: bass.AP,
    lora_bt: bass.AP,
    lin_b: bass.AP,
    gate_b: bass.AP,
    out: bass.AP,
):
    f32 = mybir.dt.float32
    f32r = mybir.dt.float32r
    i32 = mybir.dt.int32
    ALU = mybir.AluOpType
    ACT = mybir.ActivationFunctionType
    AX = mybir.AxisListType

    P = 128
    NB, C, T = x.shape
    QB = P // C
    NG = NB // QB
    KT = T // P
    R = lora_bt.shape[0]
    NR = gate_b.shape[1]
    RANKS = (8, 16, 32, 64)
    COLS = T + R + NR
    HALF = T // 2
    BANK = 512
    TAIL = COLS - HALF
    UN = 4
    LAST = NG // UN - 1

    x_rows = x.rearrange("b c t -> (b c) t")
    out_rows = out.rearrange("b c t -> (b c) t")
    w_rows = cond_w.rearrange("s c d -> (s c) d")

    ctx = ExitStack()
    with ctx:
        def sb(name, shape, dt=f32):
            return ctx.enter_context(nc.sbuf_tensor(name, shape, dt))

        def pb(name, shape):
            return ctx.enter_context(nc.psum_tensor(name, shape, f32))

        def sem(name):
            return ctx.enter_context(nc.semaphore(name))

        x_sb = [sb(f"x_sb{i}", [P, T]) for i in range(UN)]
        out_sb = [sb(f"out_sb{i}", [P, T]) for i in range(2)]
        ids = sb("ids", [P, NB], i32)
        chan = sb("chan", [P, 1], i32)
        chan_f = sb("chan_f", [P, 1])
        rows = sb("rows", [P, NG], i32)
        w_gat = [sb(f"w_gat{i}", [P, C]) for i in range(UN)]
        w_bd = [sb(f"w_bd{i}", [P, P]) for i in range(UN)]
        wag_raw = sb("wag_raw", [P, KT, COLS])
        wag_hi = sb("wag_hi", [P, KT, COLS], f32r)
        wag_lo = sb("wag_lo", [P, KT, COLS], f32r)
        bt_raw = sb("bt_raw", [P, T])
        bt_hi = sb("bt_hi", [P, T], f32r)
        bt_lo = sb("bt_lo", [P, T], f32r)
        bias_raw = sb("bias_raw", [P, T])
        bias_hi = sb("bias_hi", [P, T])
        gate_bias = sb("gate_bias", [P, NR])
        ident = sb("ident", [P, P])
        block_no = sb("block_no", [P, R])
        order = sb("order", [P, NR])
        h_hi = [sb(f"h_hi{i}", [P, T], f32r) for i in range(2)]
        h_lo = [sb(f"h_lo{i}", [P, T], f32r) for i in range(2)]
        score = sb("score", [P, NR])
        top = sb("top", [P, 1])
        shifted = [sb(f"shifted{i}", [P, NR]) for i in range(2)]
        picked = sb("picked", [P, NR])
        first = sb("first", [P, 1])
        expd = [sb(f"expd{i}", [P, NR]) for i in range(2)]
        expsum = [sb(f"expsum{i}", [P, 1]) for i in range(2)]
        inv_sum = sb("inv_sum", [P, 1])
        prob = sb("prob", [P, NR])
        prob_top = sb("prob_top", [P, 1])
        inv_top = sb("inv_top", [P, 1])
        weight = sb("weight", [P, 1])
        mask = [sb(f"mask{i}", [P, R]) for i in range(2)]
        u_raw = sb("u_raw", [P, R])
        u_sel = [sb(f"u_sel{i}", [P, 2 * R]) for i in range(2)]
        u_hilo = sb("u_hilo", [P, P], f32r)
        u_one = sb("u_one", [P, P], f32r)

        h_ps = [pb(f"h_ps{i}", [P, T]) for i in range(2)]
        acc = [pb(f"acc{i}", [P, 2 * BANK]) for i in range(2)]
        u_ps = pb("u_ps", [P, BANK])
        Y0 = BANK - HALF
        U0 = Y0 + T
        S0 = U0 + R

        wag_in = [sem(f"wag_in{k}") for k in range(KT)]
        bt_in = sem("bt_in")
        bias_in = sem("bias_in")
        gate_in = sem("gate_in")
        x_in = [sem(f"x_in{i}") for i in range(UN)]
        stored = [sem(f"stored{i}") for i in range(2)]
        ids_in = sem("ids_in")
        chan_made = sem("chan_made")
        rows_made = sem("rows_made")
        gathered = [sem(f"gathered{i}") for i in range(UN)]
        w_ready = sem("w_ready")
        zeroed = sem("zeroed")
        const_made = sem("const_made")
        u_one_made = sem("u_one_made")
        bt_zeroed = sem("bt_zeroed")
        wag_hi_made = sem("wag_hi_made")
        wag_lo_made = sem("wag_lo_made")
        bt_hi_made = sem("bt_hi_made")
        bt_lo_made = sem("bt_lo_made")
        mixed = sem("mixed")
        h_hi_made = sem("h_hi_made")
        h_lo_made = sem("h_lo_made")
        tail_done = sem("tail_done")
        main_done = sem("main_done")
        shift_made = sem("shift_made")
        exp_done = sem("exp_done")
        rank_step = sem("rank_step")
        weigh_step = sem("weigh_step")
        u_sel_made = sem("u_sel_made")
        u_turned = sem("u_turned")
        u_copied = sem("u_copied")
        y_ready = sem("y_ready")
        added = sem("added")

        def at(n, r):
            return n + r // UN, r % UN

        def count(n, r):
            return n * UN + r

        block = ctx.enter_context(nc.Block())

        @block.sync
        def _(sp):
            def load_x(n, r):
                sp.dma_start(x_sb[r][:, :], x_rows[bass.ds(count(n, r) * P, P), :]).then_inc(x_in[r], 16)

            def store(n, r):
                sp.wait_ge(added, 2 * count(n, r) + 2)
                sp.dma_start(out_rows[bass.ds(count(n, r) * P, P), :], out_sb[r % 2][:, :]).then_inc(stored[r % 2], 16)

            sp.dma_start(ids[:, :], subject.to_broadcast([P, NB])).then_inc(ids_in, 16)
            load_x(0, 0)
            for k in range(KT):
                if k == KT // 2:
                    sp.wait_ge(rows_made, QB)
                sp.dma_start(wag_raw[:, k, :], wag[k * P:(k + 1) * P, :]).then_inc(wag_in[k], 16)
            load_x(0, 1)
            sp.dma_start(gate_bias[:, :], gate_b.to_broadcast([P, NR])).then_inc(gate_in, 16)
            sp.dma_start(bt_raw[0:R, :], lora_bt[:, :]).then_inc(bt_in, 16)
            sp.dma_start(bt_raw[R:2 * R, :], lora_bt[:, :]).then_inc(bt_in, 16)
            sp.dma_start(bias_raw[64:65, :], lin_b[:, :]).then_inc(bias_in, 16)
            sp.dma_start(bias_raw[96:97, :], lin_b[:, :]).then_inc(bias_in, 16)
            load_x(0, 2)
            load_x(0, 3)
            with sp.Fori(0, LAST) as n:
                for r in range(UN):
                    store(n, r)
                    load_x(n + 1, r)
            for r in range(UN):
                store(LAST, r)
            for i in range(2):
                sp.wait_ge(stored[i], 16 * NG // 2)

        @block.gpsimd
        def _(pool):
            for q in range(QB):
                pool.iota(chan[q * C:(q + 1) * C, :], pattern=[[0, 1]], base=0, channel_multiplier=1).then_inc(chan_made, 1)
            pool.wait_ge(chan_made, QB)
            pool.memset(ident[:, :], 0.0).then_inc(const_made, 1)
            pool.wait_ge(const_made, 1)
            pool.affine_select(out=ident[:, :], in_=ident[:, :], compare_op=ALU.not_equal, fill=1.0,
                               base=0, pattern=[[-1, P]], channel_multiplier=1).then_inc(const_made, 1)
            pool.wait_ge(const_made, 2)
            pool.wait_ge(rows_made, QB)
            for g in range(NG):
                if g >= UN:
                    pool.wait_ge(w_ready, QB * (g - UN + 1))
                pool.indirect_dma_start(w_gat[g % UN][:, :], None, w_rows,
                                        bass.IndirectOffsetOnAxis(ap=rows[:, g:g + 1], axis=0)).then_inc(gathered[g % UN], 16)

        @block.scalar
        def _(act):
            def spread(n, r, reused):
                act.wait_ge(gathered[r], 16 * (n + 1))
                if reused:
                    act.wait_ge(mixed, count(n, r) - UN + 1)
                for q in range(QB):
                    s = slice(q * C, (q + 1) * C)
                    act.activation(w_bd[r][s, s], w_gat[r][s, :], ACT.Copy).then_inc(w_ready, 1)

            def weights_high(k):
                act.wait_ge(wag_in[k], 16)
                act.activation(wag_hi[:, k, :], wag_raw[:, k, :], ACT.Copy).then_inc(wag_hi_made, 1)

            def h_high(n, r, reused):
                act.wait_ge(mixed, count(n, r) + 1)
                if reused:
                    act.wait_ge(main_done, count(n, r) - 1)
                act.activation(h_hi[r % 2][:, :], h_ps[r % 2][:, :], ACT.Copy).then_inc(h_hi_made, 1)

            def exps(n, r):
                act.wait_ge(shift_made, count(n, r) + 1)
                act.activation(expd[r % 2][:, :], shifted[r % 2][:, :], ACT.Exp,
                               accum_out=expsum[r % 2][:, :]).then_inc(exp_done, 1)

            def u_out(n, r, reused):
                act.wait_ge(u_turned, count(n, r) + 1)
                if reused:
                    act.wait_ge(y_ready, 2 * count(n, r))
                act.activation(u_hilo[:, :], u_ps[:, 0:P], ACT.Copy).then_inc(u_copied, 1)
                act.activation(u_one[0:R, :], u_ps[0:R, 0:P], ACT.Copy).then_inc(u_copied, 1)

            act.wait_ge(zeroed, UN)
            weights_high(0)
            spread(0, 0, False)
            weights_high(1)
            spread(0, 1, False)
            h_high(0, 0, False)
            weights_high(2)
            weights_high(3)
            h_high(0, 1, False)
            spread(0, 2, False)
            act.wait_ge(bt_in, 32)
            act.activation(bt_hi[:, :], bt_raw[:, :], ACT.Copy).then_inc(bt_hi_made, 1)
            act.wait_ge(bias_in, 32)
            act.wait_ge(bt_zeroed, 1)
            act.activation(bt_lo[64:65, :], bias_raw[64:65, :], ACT.Copy).then_inc(bt_hi_made, 1)
            act.activation(bias_hi[96:97, :].bitcast(f32r), bias_raw[96:97, :], ACT.Copy).then_inc(bt_hi_made, 1)
            exps(0, 0)

            def slot(n, r, spread_reused, u_reused):
                h_high(*at(n, r + 1), True)
                spread(*at(n, r + 2), spread_reused)
                u_out(*at(n, r - 1), u_reused)
                exps(*at(n, r))

            slot(0, 1, False, False)
            with act.Fori(0, LAST) as n:
                for r in range(2, 2 + UN):
                    slot(n, r, True, True)
            h_high(LAST, UN - 1, True)
            u_out(LAST, UN - 3, True)
            exps(LAST, UN - 2)
            u_out(LAST, UN - 2, True)
            exps(LAST, UN - 1)
            u_out(LAST, UN - 1, True)

        @block.tensor
        def _(pe):
            def mix(n, r, reused):
                pe.wait_ge(x_in[r], 16 * (n + 1))
                pe.wait_ge(w_ready, QB * (count(n, r) + 1))
                if reused:
                    pe.wait_ge(h_lo_made, count(n, r) - 1)
                for k in range(KT):
                    mm = pe.matmul(h_ps[r % 2][:, k * P:(k + 1) * P], x_sb[r][:, k * P:(k + 1) * P], w_bd[r][:, :],
                                   start=True, stop=True)
                mm.then_inc(mixed, 1)

            BANKS = {"tail": (slice(BANK, BANK + TAIL), slice(HALF, COLS)),
                     "head": (slice(Y0, BANK), slice(0, HALF))}

            def product(r, bank, h, w, first, last, made=None):
                to, cols = BANKS[bank]
                for k in range(KT):
                    if made is not None:
                        pe.wait_ge(made, k + 1)
                    mm = pe.matmul(acc[r % 2][:, to], h[r % 2][:, k * P:(k + 1) * P], w[:, k, cols],
                                   start=first and k == 0, stop=last and k == KT - 1)
                return mm

            def main_tail(n, r, reused, fresh):
                pe.wait_ge(h_hi_made, count(n, r) + 1)
                if reused:
                    pe.wait_ge(added, 2 * count(n, r) - 3)
                product(r, "tail", h_hi, wag_hi, True, False, wag_hi_made if fresh else None)
                product(r, "tail", h_hi, wag_lo, False, False, wag_lo_made if fresh else None)
                pe.wait_ge(h_lo_made, count(n, r) + 1)
                product(r, "tail", h_lo, wag_hi, False, True).then_inc(tail_done, 1)

            def main_head_high(n, r, reused):
                if reused:
                    pe.wait_ge(added, 2 * count(n, r) - 2)
                product(r, "head", h_hi, wag_hi, True, False)

            def main_head_rest(n, r):
                product(r, "head", h_hi, wag_lo, False, False)
                product(r, "head", h_lo, wag_hi, False, True).then_inc(main_done, 1)

            def turn(n, r, reused):
                pe.wait_ge(u_sel_made, count(n, r) + 1)
                if reused:
                    pe.wait_ge(u_copied, 2 * count(n, r))
                pe.transpose(u_ps[:, 0:P], u_sel[r % 2][:, :], ident[:, :]).then_inc(u_turned, 1)

            def lora(n, r):
                pe.wait_ge(u_copied, 2 * count(n, r) + 2)
                for to, cols in ((slice(BANK, BANK + HALF), slice(HALF, T)), (slice(Y0, BANK), slice(0, HALF))):
                    for u, b in ((u_hilo, bt_hi), (u_one, bt_lo)):
                        mm = pe.matmul(acc[r % 2][:, to], u[:, :], b[:, cols], start=False, stop=False,
                                       skip_group_check=True)
                    mm.then_inc(y_ready, 1)

            mix(0, 0, False)
            mix(0, 1, False)
            main_tail(0, 0, False, True)
            main_head_high(0, 0, False)
            main_head_rest(0, 0)
            pe.wait_ge(const_made, 2)
            pe.wait_ge(bt_hi_made, 3)
            pe.wait_ge(bt_lo_made, 2)

            def slot(n, r, acc_reused, u_reused):
                mix(*at(n, r + 1), True)
                main_tail(*at(n, r), acc_reused, False)
                main_head_high(*at(n, r), acc_reused)
                turn(*at(n, r - 1), u_reused)
                main_head_rest(*at(n, r))
                lora(*at(n, r - 1))

            slot(0, 1, False, False)
            slot(0, 2, True, True)
            with pe.Fori(0, LAST) as n:
                for r in range(3, 3 + UN):
                    slot(n, r, True, True)
            main_tail(LAST, UN - 1, True, False)
            main_head_high(LAST, UN - 1, True)
            turn(LAST, UN - 2, True)
            main_head_rest(LAST, UN - 1)
            lora(LAST, UN - 2)
            turn(LAST, UN - 1, True)
            lora(LAST, UN - 1)

        @block.vector
        def _(dve):
            for i in range(UN):
                dve.memset(w_bd[i][:, :], 0.0).then_inc(zeroed, 1)
            dve.wait_ge(chan_made, QB)
            dve.tensor_copy(chan_f[:, :], chan[:, :]).then_inc(chan_made, 1)
            dve.wait_ge(chan_made, QB + 1)
            dve.wait_ge(ids_in, 16)
            for q in range(QB):
                s = slice(q * C, (q + 1) * C)
                dve.tensor_scalar(rows[s, :], ids[s, q::QB], float(C), chan_f[s, 0:1],
                                  ALU.mult, ALU.add).then_inc(rows_made, 1)
            start = 0
            for j, end in enumerate(RANKS):
                dve.memset(block_no[:, start:end], float(NR - j)).then_inc(u_one_made, 1)
                dve.memset(order[:, j:j + 1], float(NR - j)).then_inc(u_one_made, 1)
                start = end
            dve.memset(u_one[64:96, :].bitcast(f32), 0.0).then_inc(u_one_made, 1)
            dve.memset(u_one[96:128, :].bitcast(f32), 0.0).then_inc(u_one_made, 1)
            dve.wait_ge(u_one_made, 2 * NR + 2)
            dve.memset(u_one[64:65, :].bitcast(f32), 1.0).then_inc(u_one_made, 1)
            dve.memset(u_one[96:97, :].bitcast(f32), 1.0).then_inc(u_one_made, 1)
            dve.memset(bt_lo[64:128, :].bitcast(f32), 0.0).then_inc(bt_zeroed, 1)
            for k in range(KT):
                dve.wait_ge(wag_hi_made, k + 1)
                dve.tensor_tensor(wag_lo[:, k, :], wag_raw[:, k, :], wag_hi[:, k, :].bitcast(f32),
                                  ALU.subtract).then_inc(wag_lo_made, 1)

            def h_low(n, r, reused):
                dve.wait_ge(h_hi_made, count(n, r) + 1)
                if reused:
                    dve.wait_ge(main_done, count(n, r) - 1)
                dve.tensor_tensor(h_lo[r % 2][:, :], h_ps[r % 2][:, :], h_hi[r % 2][:, :].bitcast(f32),
                                  ALU.subtract).then_inc(h_lo_made, 1)

            RANK_STEPS = 5

            def rank(n, r):
                done = count(n, r) * RANK_STEPS
                dve.wait_ge(tail_done, count(n, r) + 1)
                dve.tensor_tensor(score[:, :], acc[r % 2][:, S0:S0 + NR], gate_bias[:, :],
                                  ALU.add).then_inc(rank_step, 1)
                dve.wait_ge(rank_step, done + 1)
                dve.tensor_reduce(top[:, :], score[:, :], AX.X, ALU.max).then_inc(rank_step, 1)
                dve.wait_ge(rank_step, done + 2)
                dve.tensor_scalar(shifted[r % 2][:, :], score[:, :], top[:, 0:1], None,
                                  ALU.subtract).then_inc(shift_made, 1)
                dve.wait_ge(shift_made, count(n, r) + 1)
                dve.scalar_tensor_tensor(out=picked[:, :], in0=shifted[r % 2][:, :], scalar=0.0, in1=order[:, :],
                                         op0=ALU.is_ge, op1=ALU.mult).then_inc(rank_step, 1)
                dve.wait_ge(rank_step, done + 3)
                dve.tensor_reduce(first[:, :], picked[:, :], AX.X, ALU.max).then_inc(rank_step, 1)
                dve.wait_ge(rank_step, done + 4)
                dve.tensor_scalar(mask[r % 2][:, :], block_no[:, :], first[:, 0:1], None,
                                  ALU.is_ge).then_inc(rank_step, 1)

            WEIGH_STEPS = 7

            def weigh(n, r):
                done = count(n, r) * WEIGH_STEPS
                u_ps_rows = acc[r % 2][:, U0:U0 + R]
                u = u_sel[r % 2]
                dve.wait_ge(exp_done, count(n, r) + 1)
                dve.reciprocal(inv_sum[:, :], expsum[r % 2][:, :]).then_inc(weigh_step, 1)
                dve.wait_ge(weigh_step, done + 1)
                dve.tensor_scalar(prob[:, :], expd[r % 2][:, :], inv_sum[:, 0:1], None, ALU.mult).then_inc(weigh_step, 1)
                dve.wait_ge(weigh_step, done + 2)
                dve.tensor_reduce(prob_top[:, :], prob[:, :], AX.X, ALU.max).then_inc(weigh_step, 1)
                dve.wait_ge(weigh_step, done + 3)
                dve.reciprocal(inv_top[:, :], prob_top[:, :]).then_inc(weigh_step, 1)
                dve.wait_ge(weigh_step, done + 4)
                dve.tensor_scalar(weight[:, :], prob_top[:, :], inv_top[:, 0:1], None, ALU.mult).then_inc(weigh_step, 1)
                dve.wait_ge(weigh_step, done + 5)
                dve.wait_ge(rank_step, (count(n, r) + 1) * RANK_STEPS)
                dve.scalar_tensor_tensor(out=u[:, 0:R].bitcast(f32r), in0=mask[r % 2][:, :], scalar=weight[:, 0:1],
                                         in1=u_ps_rows, op0=ALU.mult, op1=ALU.mult).then_inc(weigh_step, 1)
                dve.scalar_tensor_tensor(out=u_raw[:, :], in0=mask[r % 2][:, :], scalar=weight[:, 0:1],
                                         in1=u_ps_rows, op0=ALU.mult, op1=ALU.mult).then_inc(weigh_step, 1)
                dve.wait_ge(weigh_step, done + 7)
                dve.tensor_tensor(u[:, R:2 * R], u_raw[:, :], u[:, 0:R], ALU.subtract).then_inc(u_sel_made, 1)

            def add(n, r, reused):
                if reused:
                    dve.wait_ge(stored[r % 2], (n * (UN // 2) + r // 2) * 16)
                for half, cols in ((1, slice(HALF, T)), (2, slice(0, HALF))):
                    dve.wait_ge(y_ready, 2 * count(n, r) + half)
                    dve.tensor_tensor(out_sb[r % 2][:, cols], acc[r % 2][:, Y0 + cols.start:Y0 + cols.stop],
                                      x_sb[r][:, cols], ALU.add).then_inc(added, 1)

            h_low(0, 0, False)
            h_low(0, 1, False)
            dve.wait_ge(bt_hi_made, 3)
            dve.wait_ge(bt_zeroed, 1)
            dve.tensor_tensor(bt_lo[0:R, :], bt_raw[0:R, :], bt_hi[0:R, :].bitcast(f32), ALU.subtract).then_inc(bt_lo_made, 1)
            dve.tensor_tensor(bt_lo[96:97, :], bias_raw[96:97, :], bias_hi[96:97, :], ALU.subtract).then_inc(bt_lo_made, 1)
            dve.wait_ge(gate_in, 16)

            rank(0, 0)

            def slot(n, r, out_reused):
                weigh(*at(n, r - 1))
                h_low(*at(n, r + 1), True)
                rank(*at(n, r))
                add(*at(n, r - 1), out_reused)

            slot(0, 1, False)
            slot(0, 2, False)
            with dve.Fori(0, LAST) as n:
                for r in range(3, 3 + UN):
                    slot(n, r, True)
            weigh(LAST, UN - 2)
            rank(LAST, UN - 1)
            weigh(LAST, UN - 1)
            add(LAST, UN - 2, True)
            add(LAST, UN - 1, True)


def kernel(x, itok_B_0_30, L0_cond_weights, L0_ffn_W, L0_ffn_b, L0_ffn_A, L0_ffn_B, L0_ffn_gate_w, L0_ffn_gate_b):
    import numpy as _np
    import concourse.bacc as _bacc
    from concourse import mybir as _mybir
    from concourse.bass_utils import run_bass_kernel_spmd as _run

    w, a, g = (_np.asarray(t) for t in (L0_ffn_W, L0_ffn_A, L0_ffn_gate_w))
    laid = {
        "x": _np.asarray(x),
        "subject": _np.asarray(itok_B_0_30).reshape(1, -1),
        "cond_w": _np.asarray(L0_cond_weights),
        "wag": _np.concatenate([w.T, a.T, g.T], axis=1),
        "lora_bt": _np.asarray(L0_ffn_B).T,
        "lin_b": _np.asarray(L0_ffn_b).reshape(1, -1),
        "gate_b": _np.asarray(L0_ffn_gate_b).reshape(1, -1),
    }
    nc = _bacc.Bacc("TRN2", target_bir_lowering=False, num_devices=1)
    arrays, args = {}, []
    for name, t in laid.items():
        t = _np.ascontiguousarray(t)
        arrays[f"in_{name}_dram"] = t
        args.append(nc.dram_tensor(f"in_{name}_dram", t.shape, _mybir.dt.from_np(t.dtype), kind="ExternalInput").ap())
    args.append(nc.dram_tensor("out_0_dram", laid["x"].shape, _mybir.dt.from_np(laid["x"].dtype), kind="ExternalOutput").ap())
    bass_adaln_ffn_kernel(nc, *args)
    r = _run(nc, [arrays], core_ids=[0])
    return r.results[0]["out_0_dram"]
```

```python
import concourse.bass as bass
from concourse import mybir
from contextlib import ExitStack


def bass_adaln_ffn_kernel(
    nc: bass.Bass,
    x: bass.AP,
    subject: bass.AP,
    cond_w: bass.AP,
    wag: bass.AP,
    lora_b: bass.AP,
    gate_b: bass.AP,
    out: bass.AP,
):
    f32 = mybir.dt.float32
    f32r = mybir.dt.float32r
    i32 = mybir.dt.int32
    ALU = mybir.AluOpType
    ACT = mybir.ActivationFunctionType
    AX = mybir.AxisListType

    P = 128
    NB, C, T = x.shape
    QB = P // C
    NG = NB // QB
    KT = T // P
    R = wag.shape[1] - T - gate_b.shape[1]
    NR = gate_b.shape[1]
    RANKS = (8, 16, 32, 64)
    BIAS_HI, BIAS_LO = 64, 96
    COLS = T + R + NR
    HALF = T // 2
    BANK = 512
    TAIL = COLS - HALF
    UN = 4
    LAST = NG // UN - 1
    WARM = 12

    x_rows = x.rearrange("b c t -> (b c) t")
    out_rows = out.rearrange("b c t -> (b c) t")
    w_rows = cond_w.rearrange("s c d -> (s c) d")

    ctx = ExitStack()
    with ctx:
        def sb(name, shape, dt=f32):
            return ctx.enter_context(nc.sbuf_tensor(name, shape, dt))

        def pb(name, shape):
            return ctx.enter_context(nc.psum_tensor(name, shape, f32))

        def sem(name):
            return ctx.enter_context(nc.semaphore(name))

        x_sb = [sb(f"x_sb{i}", [P, T]) for i in range(UN)]
        out_sb = [sb(f"out_sb{i}", [P, T]) for i in range(2)]
        ids = sb("ids", [P, NG], i32)
        chan = sb("chan", [P, 1], i32)
        chan_f = sb("chan_f", [P, 1])
        rows = sb("rows", [P, NG], i32)
        w_gat = [sb(f"w_gat{i}", [P, C]) for i in range(UN)]
        w_bd = [sb(f"w_bd{i}", [P, P]) for i in range(UN)]
        wag_raw = sb("wag_raw", [P, KT, COLS])
        wag_hi = sb("wag_hi", [P, KT, COLS], f32r)
        wag_lo = sb("wag_lo", [P, KT, COLS], f32r)
        lb_raw = sb("lb_raw", [P, T])
        lb_sub = sb("lb_sub", [P, T])
        bt_hi = sb("bt_hi", [P, T], f32r)
        bt_lo = sb("bt_lo", [P, T], f32r)
        gate_bias = sb("gate_bias", [P, NR])
        ident = sb("ident", [P, P])
        set_limit = sb("set_limit", [P, R])
        set_bit = sb("set_bit", [P, NR])
        h_hi = [sb(f"h_hi{i}", [P, T], f32r) for i in range(UN)]
        h_lo = [sb(f"h_lo{i}", [P, T], f32r) for i in range(UN)]
        neg_score = sb("neg_score", [P, NR])
        neg_top = sb("neg_top", [P, 1])
        picked = sb("picked", [P, NR])
        chosen = sb("chosen", [P, 1])
        expd = sb("expd", [P, NR])
        expsum = sb("expsum", [P, 1])
        inv_sum = sb("inv_sum", [P, 1])
        exp_top = sb("exp_top", [P, 1])
        prob_top = sb("prob_top", [P, 1])
        inv_top = sb("inv_top", [P, 1])
        u_kept = sb("u_kept", [P, R])
        u_prob = sb("u_prob", [P, R])
        u_sel = [sb(f"u_sel{i}", [P, 2 * R]) for i in range(2)]
        u_hilo = sb("u_hilo", [P, P], f32r)
        u_one = sb("u_one", [P, P], f32r)

        h_ps = [pb(f"h_ps{i}", [P, T]) for i in range(2)]
        acc = [pb(f"acc{i}", [P, 2 * BANK]) for i in range(2)]
        u_ps = pb("u_ps", [P, BANK])
        Y0 = BANK - HALF
        U0 = Y0 + T
        S0 = U0 + R

        wag_in = [sem(f"wag_in{k}") for k in range(KT)]
        lb_in = sem("lb_in")
        gate_in = sem("gate_in")
        x_in = [sem(f"x_in{i}") for i in range(UN)]
        stored = [sem(f"stored{i}") for i in range(2)]
        last_stored = sem("last_stored")
        ids_in = sem("ids_in")
        chan_made = sem("chan_made")
        rows_made = sem("rows_made")
        gathered = [sem(f"gathered{i}") for i in range(UN)]
        w_ready = sem("w_ready")
        zeroed = sem("zeroed")
        ident_made = sem("ident_made")
        sets_made = sem("sets_made")
        u_one_zeroed = sem("u_one_zeroed")
        u_one_set = sem("u_one_set")
        wag_hi_made = sem("wag_hi_made")
        wag_lo_made = sem("wag_lo_made")
        bt_hi_made = sem("bt_hi_made")
        bt_lo_made = sem("bt_lo_made")
        mixed = sem("mixed")
        h_hi_made = sem("h_hi_made")
        h_lo_made = sem("h_lo_made")
        tail_done = sem("tail_done")
        main_done = sem("main_done")
        top_made = sem("top_made")
        exp_done = sem("exp_done")
        rank_step = sem("rank_step")
        weigh_step = sem("weigh_step")
        u_sel_made = sem("u_sel_made")
        u_turned = sem("u_turned")
        u_copied = sem("u_copied")
        y_ready = sem("y_ready")
        added = sem("added")

        def at(n, r):
            return n + r // UN, r % UN

        def count(n, r):
            return n * UN + r

        block = ctx.enter_context(nc.Block())

        @block.sync
        def _(sp):
            def load_x(n, r):
                sp.dma_start(x_sb[r][:, :], x_rows[bass.ds(count(n, r) * P, P), :]).then_inc(x_in[r], 16)

            def store(n, r):
                sp.wait_ge(added, 2 * count(n, r) + 2)
                sp.dma_start(out_rows[bass.ds(count(n, r) * P, P), :], out_sb[r % 2][:, :]).then_inc(stored[r % 2], 16)

            def load_wag(k):
                sp.dma_start(wag_raw[:, k, :], wag[k * P:(k + 1) * P, :]).then_inc(wag_in[k], 16)

            sp.dma_start(ids[:, :], subject.unsqueeze(1).broadcast_to([QB, C, NG])).then_inc(ids_in, 16)
            for k in range(KT - 1):
                load_wag(k)
            load_x(0, 0)
            sp.wait_ge(wag_in[1], 16)
            load_x(0, 1)
            load_wag(KT - 1)
            sp.dma_start(lb_raw[:, :], lora_b[:, :]).then_inc(lb_in, 16)
            sp.dma_start(gate_bias[:, :], gate_b.to_broadcast([P, NR])).then_inc(gate_in, 16)
            load_x(0, 2)
            load_x(0, 3)
            with sp.Fori(0, LAST) as n:
                for r in range(UN):
                    store(n, r)
                    load_x(n + 1, r)
            for r in range(UN - 1):
                store(LAST, r)
            for half, cols in ((1, slice(HALF, T)), (2, slice(0, HALF))):
                sp.wait_ge(added, 2 * (NG - 1) + half)
                sp.dma_start(out_rows[(NG - 1) * P:NG * P, cols], out_sb[(NG - 1) % 2][:, cols]).then_inc(last_stored, 16)
            for i in range(2):
                sp.wait_ge(stored[i], 16 * (NG // 2 - (i == (NG - 1) % 2)))
            sp.wait_ge(last_stored, 32)

        @block.gpsimd
        def _(pool):
            for q in range(QB):
                pool.iota(chan[q * C:(q + 1) * C, :], pattern=[[0, 1]], base=0, channel_multiplier=1).then_inc(chan_made, 1)
            pool.wait_ge(chan_made, QB)
            pool.memset(ident[:, :], 0.0).then_inc(ident_made, 1)
            pool.wait_ge(ident_made, 1)
            pool.affine_select(out=ident[:, :], in_=ident[:, :], compare_op=ALU.not_equal, fill=1.0,
                               base=0, pattern=[[-1, P]], channel_multiplier=1).then_inc(ident_made, 1)
            pool.wait_ge(ident_made, 2)
            pool.wait_ge(rows_made, 1)
            for g in range(NG):
                if g >= UN:
                    pool.wait_ge(w_ready, QB * (g - UN + 1))
                pool.indirect_dma_start(w_gat[g % UN][:, :], None, w_rows,
                                        bass.IndirectOffsetOnAxis(ap=rows[:, g:g + 1], axis=0)).then_inc(gathered[g % UN], 16)

        @block.scalar
        def _(act):
            def spread(n, r, reused):
                act.wait_ge(gathered[r], 16 * (n + 1))
                if reused:
                    act.wait_ge(mixed, count(n, r) - UN + 1)
                for q in range(QB):
                    s = slice(q * C, (q + 1) * C)
                    act.activation(w_bd[r][s, s], w_gat[r][s, :], ACT.Copy).then_inc(w_ready, 1)

            def weights_high(k):
                act.wait_ge(wag_in[k], 16)
                act.activation(wag_hi[:, k, :], wag_raw[:, k, :], ACT.Copy).then_inc(wag_hi_made, 1)

            def h_high(n, r, reused):
                act.wait_ge(mixed, count(n, r) + 1)
                if reused:
                    act.wait_ge(main_done, count(n, r) - 2)
                act.activation(h_hi[r][:, :], h_ps[r % 2][:, :], ACT.Copy).then_inc(h_hi_made, 1)

            def exps(n, r):
                act.wait_ge(top_made, count(n, r) + 1)
                act.activation(expd[:, :], neg_score[:, :], ACT.Exp, bias=neg_top[:, 0:1], scale=-1.0,
                               accum_out=expsum[:, :]).then_inc(exp_done, 1)

            def u_out(n, r, reused):
                act.wait_ge(u_turned, count(n, r) + 1)
                if reused:
                    act.wait_ge(y_ready, 2 * count(n, r))
                act.activation(u_hilo[:, :], u_ps[:, 0:P], ACT.Copy).then_inc(u_copied, 1)
                act.activation(u_one[0:R, :], u_ps[0:R, 0:P], ACT.Copy).then_inc(u_copied, 1)

            act.wait_ge(zeroed, UN)
            act.activation(u_one[R:P, :], w_bd[UN - 1][R:P, :], ACT.Copy).then_inc(u_one_zeroed, 1)
            weights_high(0)
            weights_high(1)
            weights_high(2)
            act.wait_ge(gathered[0], 16)
            for q in range(QB // 2, QB):
                s = slice(q * C, (q + 1) * C)
                act.activation(w_bd[0][s, s], w_gat[0][s, :], ACT.Copy).then_inc(w_ready, 1)
            h_high(0, 0, False)
            weights_high(3)
            h_high(0, 1, False)
            spread(0, 2, False)
            act.wait_ge(lb_in, 16)
            act.activation(bt_hi[0:R, :], lb_raw[0:R, :], ACT.Copy).then_inc(bt_hi_made, 1)
            act.activation(bt_hi[R:P, :], lb_raw[0:R, :], ACT.Copy).then_inc(bt_hi_made, 1)
            act.activation(lb_sub[BIAS_LO:P, :].bitcast(f32r), lb_raw[BIAS_LO:P, :], ACT.Copy).then_inc(bt_hi_made, 1)
            exps(0, 0)
            act.activation(lb_sub[0:R, :].bitcast(f32r), lb_raw[0:R, :], ACT.Copy).then_inc(bt_hi_made, 1)

            def slot(n, r, h_reused, spread_reused, u_reused):
                h_high(*at(n, r + 1), h_reused)
                spread(*at(n, r + 2), spread_reused)
                u_out(*at(n, r - 1), u_reused)
                exps(*at(n, r))

            slot(0, 1, False, False, False)
            with act.Fori(0, LAST) as n:
                for r in range(2, 2 + UN):
                    slot(n, r, True, True, True)
            h_high(LAST, UN - 1, True)
            u_out(LAST, UN - 3, True)
            exps(LAST, UN - 2)
            u_out(LAST, UN - 2, True)
            exps(LAST, UN - 1)
            u_out(LAST, UN - 1, True)

        @block.tensor
        def _(pe):
            def mix(n, r, reused):
                pe.wait_ge(x_in[r], 16 * (n + 1))
                pe.wait_ge(w_ready, QB * (count(n, r) + 1))
                if reused:
                    pe.wait_ge(h_lo_made, count(n, r) - 1)
                for k in range(KT):
                    mm = pe.matmul(h_ps[r % 2][:, k * P:(k + 1) * P], x_sb[r][:, k * P:(k + 1) * P], w_bd[r][:, :],
                                   start=True, stop=True)
                mm.then_inc(mixed, 1)

            BANKS = {"tail": (slice(BANK, BANK + TAIL), slice(HALF, COLS)),
                     "head": (slice(Y0, BANK), slice(0, HALF))}

            def product(r, bank, h, w, first, last, made=None):
                to, cols = BANKS[bank]
                for k in range(KT):
                    if made is not None:
                        pe.wait_ge(made, k + 1)
                    mm = pe.matmul(acc[r % 2][:, to], h[r][:, k * P:(k + 1) * P], w[:, k, cols],
                                   start=first and k == 0, stop=last and k == KT - 1)
                return mm

            def main_tail_high(n, r, reused):
                pe.wait_ge(h_hi_made, count(n, r) + 1)
                if reused:
                    pe.wait_ge(added, 2 * count(n, r) - 3)
                product(r, "tail", h_hi, wag_hi, True, False)
                product(r, "tail", h_hi, wag_lo, False, False)

            def main_tail_low(n, r):
                pe.wait_ge(h_lo_made, count(n, r) + 1)
                product(r, "tail", h_lo, wag_hi, False, True).then_inc(tail_done, 1)

            def main_head_high(n, r, reused):
                if reused:
                    pe.wait_ge(added, 2 * count(n, r) - 2)
                product(r, "head", h_hi, wag_hi, True, False)
                product(r, "head", h_hi, wag_lo, False, False)

            def main_head_low(n, r):
                product(r, "head", h_lo, wag_hi, False, True).then_inc(main_done, 1)

            def turn(n, r, reused):
                pe.wait_ge(u_sel_made, count(n, r) + 1)
                if reused:
                    pe.wait_ge(u_copied, 2 * count(n, r))
                pe.transpose(u_ps[:, 0:P], u_sel[r % 2][:, :], ident[:, :]).then_inc(u_turned, 1)

            def lora(n, r):
                for to, cols in ((slice(BANK, BANK + HALF), slice(HALF, T)), (slice(Y0, BANK), slice(0, HALF))):
                    for copies, (u, b) in enumerate(((u_hilo, bt_hi), (u_one, bt_lo))):
                        if cols.start == HALF:
                            pe.wait_ge(u_copied, 2 * count(n, r) + 1 + copies)
                        mm = pe.matmul(acc[r % 2][:, to], u[:, :], b[:, cols], start=False, stop=False,
                                       skip_group_check=True)
                    mm.then_inc(y_ready, 1)

            pe.wait_ge(ident_made, 2)
            for _ in range(WARM):
                pe.matmul(acc[1][:, 0:P], ident[:, :], ident[:, :], start=True, stop=True)
            mix(0, 0, False)
            mix(0, 1, False)
            pe.wait_ge(h_hi_made, 1)
            product(0, "tail", h_hi, wag_hi, True, False, wag_hi_made)
            product(0, "head", h_hi, wag_hi, True, False)
            product(0, "tail", h_hi, wag_lo, False, False, wag_lo_made)
            pe.wait_ge(h_lo_made, 1)
            product(0, "tail", h_lo, wag_hi, False, True).then_inc(tail_done, 1)
            product(0, "head", h_hi, wag_lo, False, False)

            def slot(n, r, acc_reused, u_reused):
                mix(*at(n, r + 1), True)
                main_tail_high(*at(n, r), acc_reused)
                turn(*at(n, r - 1), u_reused)
                main_tail_low(*at(n, r))
                main_head_low(*at(n, r - 1))
                lora(*at(n, r - 1))
                main_head_high(*at(n, r), acc_reused)

            mix(0, 2, True)
            main_tail_high(0, 1, False)
            turn(0, 0, False)
            main_tail_low(0, 1)
            main_head_low(0, 0)
            pe.wait_ge(bt_hi_made, 4)
            pe.wait_ge(bt_lo_made, 1)
            pe.wait_ge(u_one_set, 2)
            lora(0, 0)
            main_head_high(0, 1, False)
            slot(0, 2, True, True)
            with pe.Fori(0, LAST) as n:
                for r in range(3, 3 + UN):
                    slot(n, r, True, True)
            main_tail_high(LAST, UN - 1, True)
            main_tail_low(LAST, UN - 1)
            turn(LAST, UN - 2, True)
            main_head_high(LAST, UN - 1, True)
            main_head_low(LAST, UN - 2)
            lora(LAST, UN - 2)
            turn(LAST, UN - 1, True)
            main_head_low(LAST, UN - 1)
            lora(LAST, UN - 1)

        @block.vector
        def _(dve):
            for i in range(UN):
                dve.memset(w_bd[i][:, :], 0.0).then_inc(zeroed, 1)
            dve.wait_ge(chan_made, QB)
            dve.tensor_copy(chan_f[:, :], chan[:, :]).then_inc(chan_made, 1)
            start = 0
            for j, end in enumerate(RANKS):
                dve.memset(set_limit[:, start:end], float(2 ** (NR - j))).then_inc(sets_made, 1)
                dve.memset(set_bit[:, j:j + 1], float(2 ** (NR - 1 - j))).then_inc(sets_made, 1)
                start = end
            dve.memset(lb_sub[BIAS_HI:BIAS_LO, :], 0.0).then_inc(sets_made, 1)
            dve.wait_ge(u_one_zeroed, 1)
            dve.memset(u_one[BIAS_HI:BIAS_HI + 1, :].bitcast(f32), 1.0).then_inc(u_one_set, 1)
            dve.memset(u_one[BIAS_LO:BIAS_LO + 1, :].bitcast(f32), 1.0).then_inc(u_one_set, 1)
            dve.wait_ge(chan_made, QB + 1)
            dve.wait_ge(ids_in, 16)
            dve.tensor_scalar(rows[:, :], ids[:, :], float(C), chan_f[:, 0:1], ALU.mult, ALU.add).then_inc(rows_made, 1)

            def h_low(n, r, reused):
                dve.wait_ge(h_hi_made, count(n, r) + 1)
                if reused:
                    dve.wait_ge(main_done, count(n, r) - 2)
                dve.tensor_tensor(h_lo[r][:, :], h_ps[r % 2][:, :], h_hi[r][:, :].bitcast(f32),
                                  ALU.subtract).then_inc(h_lo_made, 1)

            for k in range(KT):
                if k == 2:
                    dve.wait_ge(gathered[0], 16)
                    for q in range(QB // 2):
                        s = slice(q * C, (q + 1) * C)
                        dve.tensor_copy(w_bd[0][s, s], w_gat[0][s, :]).then_inc(w_ready, 1)
                if k == KT - 1:
                    dve.wait_ge(gathered[1], 16)
                    dve.wait_ge(w_ready, QB)
                    for q in range(QB):
                        s = slice(q * C, (q + 1) * C)
                        dve.tensor_copy(w_bd[1][s, s], w_gat[1][s, :]).then_inc(w_ready, 1)
                    h_low(0, 0, False)
                dve.wait_ge(wag_hi_made, k + 1)
                dve.tensor_tensor(wag_lo[:, k, :], wag_raw[:, k, :], wag_hi[:, k, :].bitcast(f32),
                                  ALU.subtract).then_inc(wag_lo_made, 1)

            RANK_STEPS = 3

            def rank(n, r):
                done = count(n, r) * RANK_STEPS
                dve.wait_ge(tail_done, count(n, r) + 1)
                dve.scalar_tensor_tensor(out=neg_score[:, :], in0=acc[r % 2][:, S0:S0 + NR], scalar=-1.0,
                                         in1=gate_bias[:, :], op0=ALU.mult, op1=ALU.subtract).then_inc(rank_step, 1)
                dve.wait_ge(rank_step, done + 1)
                dve.tensor_reduce(neg_top[:, :], neg_score[:, :], AX.X, ALU.min).then_inc(top_made, 1)
                dve.wait_ge(top_made, count(n, r) + 1)
                dve.scalar_tensor_tensor(out=picked[:, :], in0=neg_score[:, :], scalar=neg_top[:, 0:1],
                                         in1=set_bit[:, :], op0=ALU.is_le, op1=ALU.mult,
                                         accum_out=chosen[:, :]).then_inc(rank_step, 1)
                dve.wait_ge(rank_step, done + 2)
                dve.scalar_tensor_tensor(out=u_kept[:, :], in0=set_limit[:, :], scalar=chosen[:, 0:1],
                                         in1=acc[r % 2][:, U0:U0 + R], op0=ALU.is_gt, op1=ALU.mult).then_inc(rank_step, 1)

            WEIGH_STEPS = 6

            def weigh(n, r):
                done = count(n, r) * WEIGH_STEPS
                u = u_sel[r % 2]
                dve.wait_ge(exp_done, count(n, r) + 1)
                dve.reciprocal(inv_sum[:, :], expsum[:, :]).then_inc(weigh_step, 1)
                dve.tensor_reduce(exp_top[:, :], expd[:, :], AX.X, ALU.max).then_inc(weigh_step, 1)
                dve.wait_ge(weigh_step, done + 2)
                dve.tensor_scalar(prob_top[:, :], exp_top[:, :], inv_sum[:, 0:1], None, ALU.mult).then_inc(weigh_step, 1)
                dve.wait_ge(weigh_step, done + 3)
                dve.reciprocal(inv_top[:, :], prob_top[:, :]).then_inc(weigh_step, 1)
                dve.wait_ge(rank_step, (count(n, r) + 1) * RANK_STEPS)
                dve.tensor_scalar(u_prob[:, :], u_kept[:, :], prob_top[:, 0:1], None, ALU.mult).then_inc(weigh_step, 1)
                dve.wait_ge(weigh_step, done + 5)
                dve.tensor_scalar(u[:, 0:R].bitcast(f32r), u_prob[:, :], inv_top[:, 0:1], None,
                                  ALU.mult).then_inc(weigh_step, 1)
                dve.wait_ge(weigh_step, done + 6)
                dve.scalar_tensor_tensor(out=u[:, R:2 * R], in0=u_prob[:, :], scalar=inv_top[:, 0:1], in1=u[:, 0:R],
                                         op0=ALU.mult, op1=ALU.subtract).then_inc(u_sel_made, 1)

            def add(n, r, reused):
                if reused:
                    dve.wait_ge(stored[r % 2], (n * (UN // 2) + r // 2) * 16)
                for half, cols in ((1, slice(HALF, T)), (2, slice(0, HALF))):
                    dve.wait_ge(y_ready, 2 * count(n, r) + half)
                    dve.tensor_tensor(out_sb[r % 2][:, cols], acc[r % 2][:, Y0 + cols.start:Y0 + cols.stop],
                                      x_sb[r][:, cols], ALU.add).then_inc(added, 1)

            h_low(0, 1, False)
            dve.wait_ge(gate_in, 16)
            rank(0, 0)

            def slot(n, r, h_reused, out_reused):
                h_low(*at(n, r + 1), h_reused)
                rank(*at(n, r))
                add(*at(n, r - 1), out_reused)
                weigh(*at(n, r))

            weigh(0, 0)
            dve.wait_ge(bt_hi_made, 4)
            dve.wait_ge(sets_made, 2 * NR + 1)
            dve.tensor_tensor(bt_lo[:, :], lb_raw[:, :], lb_sub[:, :], ALU.subtract).then_inc(bt_lo_made, 1)
            slot(0, 1, False, False)
            slot(0, 2, True, False)
            with dve.Fori(0, LAST) as n:
                for r in range(3, 3 + UN):
                    slot(n, r, True, True)
            rank(LAST, UN - 1)
            weigh(LAST, UN - 1)
            add(LAST, UN - 2, True)
            add(LAST, UN - 1, True)


def kernel(x, itok_B_0_30, L0_cond_weights, L0_ffn_W, L0_ffn_b, L0_ffn_A, L0_ffn_B, L0_ffn_gate_w, L0_ffn_gate_b):
    import numpy as _np
    import concourse.bacc as _bacc
    from concourse import mybir as _mybir
    from concourse.bass_utils import run_bass_kernel_spmd as _run

    w, a, g = (_np.asarray(t) for t in (L0_ffn_W, L0_ffn_A, L0_ffn_gate_w))
    bt, b = _np.asarray(L0_ffn_B).T, _np.asarray(L0_ffn_b).reshape(1, -1)
    quadrant = 32
    gap = _np.zeros((quadrant - 1, b.shape[1]), b.dtype)
    lora_b = _np.concatenate([bt, b, gap, b, gap], axis=0)
    batches = 128 // x.shape[1]
    subject = _np.asarray(itok_B_0_30).reshape(-1, batches).T
    laid = {
        "x": _np.asarray(x),
        "subject": subject,
        "cond_w": _np.asarray(L0_cond_weights),
        "wag": _np.concatenate([w.T, a.T, g.T], axis=1),
        "lora_b": lora_b,
        "gate_b": _np.asarray(L0_ffn_gate_b).reshape(1, -1),
    }
    nc = _bacc.Bacc("TRN2", target_bir_lowering=False, num_devices=1)
    arrays, args = {}, []
    for name, t in laid.items():
        t = _np.ascontiguousarray(t)
        arrays[f"in_{name}_dram"] = t
        args.append(nc.dram_tensor(f"in_{name}_dram", t.shape, _mybir.dt.from_np(t.dtype), kind="ExternalInput").ap())
    args.append(nc.dram_tensor("out_0_dram", laid["x"].shape, _mybir.dt.from_np(laid["x"].dtype), kind="ExternalOutput").ap())
    bass_adaln_ffn_kernel(nc, *args)
    r = _run(nc, [arrays], core_ids=[0])
    return r.results[0]["out_0_dram"]
```
